# Optimizing a Trainium2 kernel written in Bass

```python
import numpy as np
import jax
import jax.numpy as jnp

def _softmax(x, axis=-1):
    return jax.nn.softmax(x, axis=axis)

def _gelu(x):
    return jax.nn.gelu(x, approximate=True)

def _silu(x):
    return jax.nn.silu(x)

def _sigmoid(x):
    return jax.nn.sigmoid(x)

def _layernorm(x, axis=-1, eps=1e-05):
    m = jnp.mean(x, axis=axis, keepdims=True)
    v = jnp.var(x, axis=axis, keepdims=True)
    return (x - m) / jnp.sqrt(v + eps)

def _scatter_add(tgt, idx, src, axis=0):
    return tgt.at[idx].add(src)

def _segment_sum(src, seg, n):
    return jax.ops.segment_sum(src, seg, n)
kernel_name = 'mk_rec_standalone_d1_rec_r8_8fae0b'

def setup_inputs(seed: int=0):
    np.random.seed(seed)
    _w = jnp.asarray

    def _rec_inputs():
        import jax
        import jax.numpy as jnp
        _rk = jax.random.key(seed)
        r_field_vectors = -7.10856e-05 + 0.999911 * jax.random.normal(jax.random.fold_in(_rk, 1), (512, 8, 1024), jnp.float32)
        return r_field_vectors
    r_field_vectors = _rec_inputs()

    def _L0_rec_setup():
        import jax, jax.numpy as jnp
        import numpy as np
        B, F, H = (1024, 8, 1024)

        def _linear_params(key, fan_in, fan_out):
            kw, kb = jax.random.split(key)
            w = jax.random.normal(kw, (fan_in, fan_out), dtype=jnp.float32) * 0.02
            b = jax.random.normal(kb, (fan_out,), dtype=jnp.float32) * 0.02
            return (w, b)
        key = jax.random.key(seed)
        ks = jax.random.split(key, 7)
        field_vectors = jax.random.normal(ks[0], (B, F, H), dtype=jnp.float32)
        Wn1, bn1 = _linear_params(ks[1], H, H)
        Wn2, bn2 = _linear_params(ks[2], H, H)
        Wa1, ba1 = _linear_params(ks[3], 2 * H, H)
        Wa2, ba2 = _linear_params(ks[4], H, H)
        Wo1, bo1 = _linear_params(ks[5], 2 * H, H)
        Wo2, bo2 = _linear_params(ks[6], H, H)
        not_idx = jnp.array([2, 3], dtype=jnp.int64)
        and_pairs = jnp.array([[0, 1], [2, 3]], dtype=jnp.int64)
        or_pairs = jnp.array([[4, 5]], dtype=jnp.int64)
        return {'field_vectors': field_vectors, 'Wn1': Wn1, 'bn1': bn1, 'Wn2': Wn2, 'bn2': bn2, 'Wa1': Wa1, 'ba1': ba1, 'Wa2': Wa2, 'ba2': ba2, 'Wo1': Wo1, 'bo1': bo1, 'Wo2': Wo2, 'bo2': bo2, 'not_idx': not_idx, 'and_pairs': and_pairs, 'or_pairs': or_pairs}
    _L0_rec_all = _L0_rec_setup()
    _L0_rec_in = {k: v for k, v in _L0_rec_all.items() if k in ('Wn1', 'bn1', 'Wn2', 'bn2', 'Wa1', 'ba1', 'Wa2', 'ba2', 'Wo1', 'bo1', 'Wo2', 'bo2', 'not_idx', 'and_pairs', 'or_pairs')}
    del _L0_rec_all
    return {'r_field_vectors': r_field_vectors, 'L0_rec_Wn1': _L0_rec_in['Wn1'], 'L0_rec_bn1': _L0_rec_in['bn1'], 'L0_rec_Wn2': _L0_rec_in['Wn2'], 'L0_rec_bn2': _L0_rec_in['bn2'], 'L0_rec_Wa1': _L0_rec_in['Wa1'], 'L0_rec_ba1': _L0_rec_in['ba1'], 'L0_rec_Wa2': _L0_rec_in['Wa2'], 'L0_rec_ba2': _L0_rec_in['ba2'], 'L0_rec_Wo1': _L0_rec_in['Wo1'], 'L0_rec_bo1': _L0_rec_in['bo1'], 'L0_rec_Wo2': _L0_rec_in['Wo2'], 'L0_rec_bo2': _L0_rec_in['bo2'], 'L0_rec_not_idx': _L0_rec_in['not_idx'], 'L0_rec_and_pairs': _L0_rec_in['and_pairs'], 'L0_rec_or_pairs': _L0_rec_in['or_pairs']}

def reference(r_field_vectors, L0_rec_Wn1, L0_rec_bn1, L0_rec_Wn2, L0_rec_bn2, L0_rec_Wa1, L0_rec_ba1, L0_rec_Wa2, L0_rec_ba2, L0_rec_Wo1, L0_rec_bo1, L0_rec_Wo2, L0_rec_bo2, L0_rec_not_idx, L0_rec_and_pairs, L0_rec_or_pairs):
    import jax
    import jax.numpy as jnp

    def _L0_rec_ref(field_vectors, Wn1, bn1, Wn2, bn2, Wa1, ba1, Wa2, ba2, Wo1, bo1, Wo2, bo2, not_idx, and_pairs, or_pairs):
        import jax, jax.numpy as jnp
        import numpy as np
        B, F, H = (1024, 8, 1024)

        def _linear_params(key, fan_in, fan_out):
            kw, kb = jax.random.split(key)
            w = jax.random.normal(kw, (fan_in, fan_out), dtype=jnp.float32) * 0.02
            b = jax.random.normal(kb, (fan_out,), dtype=jnp.float32) * 0.02
            return (w, b)
        num_fields = field_vectors.shape[1]
        x_not = jnp.take(field_vectors, not_idx, axis=1)
        t = jnp.tanh(jax.nn.relu(x_not @ Wn1 + bn1) @ Wn2 + bn2)
        iv = field_vectors.at[:, not_idx, :].set(t)

        def pair_fuse(pairs, W1, b1, W2, b2):
            v = jnp.concatenate([jnp.take(iv, pairs[:, 0], axis=1), jnp.take(iv, pairs[:, 1], axis=1)], axis=-1)
            return jax.nn.relu(v @ W1 + b1) @ W2 + b2
        and_out = pair_fuse(and_pairs, Wa1, ba1, Wa2, ba2)
        or_out = pair_fuse(or_pairs, Wo1, bo1, Wo2, bo2)
        processed = jnp.zeros((num_fields,), dtype=field_vectors.dtype).at[and_pairs.reshape(-1)].set(1.0).at[or_pairs.reshape(-1)].set(1.0)
        remaining = 1.0 - processed
        sum_res = and_out.sum(axis=1) + or_out.sum(axis=1) + jnp.einsum('bfh,f->bh', iv, remaining)
        count = and_pairs.shape[0] + or_pairs.shape[0] + remaining.sum()
        return sum_res / count
    y = _L0_rec_ref(r_field_vectors, L0_rec_Wn1, L0_rec_bn1, L0_rec_Wn2, L0_rec_bn2, L0_rec_Wa1, L0_rec_ba1, L0_rec_Wa2, L0_rec_ba2, L0_rec_Wo1, L0_rec_bo1, L0_rec_Wo2, L0_rec_bo2, L0_rec_not_idx, L0_rec_and_pairs, L0_rec_or_pairs)
    return y

_drawn_inputs = setup_inputs


def setup_inputs(seed=0):
    import zlib

    import numpy as np

    out = dict(_drawn_inputs(seed))
    spreads = {}
    factors = {'L0_rec_bn1': 27.146,
     'L0_rec_bn2': 8.0,
     'L0_rec_ba1': 5.496,
     'L0_rec_bo1': 8.0,
     'L0_rec_bo2': 4.238}
    for name, (base, spread) in spreads.items():
        noise = np.random.default_rng([zlib.crc32(name.encode()), seed]).standard_normal(out[name].shape)
        drawn = base * np.exp(spread * noise) if base else spread * noise
        out[name] = jnp.asarray(drawn.astype(out[name].dtype))
    for name, factor in factors.items():
        out[name] = (out[name] * factor).astype(out[name].dtype)
    return out
```

```python
import numpy as np
import concourse.bass as bass
import concourse.mybir as mybir

F32 = mybir.dt.float32
F32R = mybir.dt.float32r
I32 = mybir.dt.int32
ALU = mybir.AluOpType
ACT = mybir.ActivationFunctionType
AX = mybir.AxisListType

P = 128
Q = 32
NQ = P // Q
FIELDS = 8
H = 1024
B = 512
BLK = H // P
JB = B // Q
SPAN = H // NQ
HALF = H // 2
HB = BLK // 2
LAND = SPAN // 2
DMA = 16
PAIR = 4 * DMA

NOT_UNITS = 2 * BLK
AND0 = 2 * NOT_UNITS
OR0 = AND0 + 4 * BLK
OUT0 = OR0 + 4 * BLK
UNITS = OUT0 + 4 * BLK
X_AND0 = 2 * AND0
X_OR0 = 2 * OR0
X_OUT0 = X_OR0 + 2 * BLK
BANKS = 8
GROUPS_2 = 6
FREE0 = BANKS


def ne(a, b):
    return (((a - b) & (FIELDS - 1)) + FIELDS - 1) >> 3


class Slots:

    made = 0

    def __init__(self, eng, not_idx):
        self.eng = eng
        self.n0 = self.index(not_idx[:, 0:1])
        self.n1 = self.index(not_idx[:, 1:2])
        differ = ne(self.n0, self.n1)
        self.second = self.small(differ)
        self.p1 = self.small(self.swap0(self.n1) + 1 - differ)

    def small(self, v):
        Slots.made += 1
        reg = self.eng.alloc_register(f"slots_{Slots.made}")
        self.eng.reg_mov(reg, v)
        return self.eng.snap(reg, min_val=0, max_val=FIELDS - 1)

    def index(self, ap):
        return self.small(self.eng.value_load(ap) & (FIELDS - 1))

    def swap0(self, f):
        return self.small(f * ne(f, self.n0) + self.n0 * (1 - ne(f, 0)))

    def swap1(self, x):
        return self.small(x + (self.p1 - 1) * (ne(x, self.p1) - ne(x, 1)))

    def slot(self, field):
        return self.swap1(self.swap0(field))

    def field(self, slot):
        return self.swap0(self.swap1(slot))


def build(nc, x, wn1, bn1, wn2, bn2, wa1, ba1, wa2, ba2, wo1, bo1, wo2, bo2,
          not_idx, and_pairs, or_pairs, out):
    not_idx = not_idx.rearrange("(o n) -> o n", o=1)
    xt = nc.alloc_sbuf_tensor("fields_t", [P, FIELDS * BLK, B], F32).ap()
    hid = nc.alloc_sbuf_tensor("hidden_t", [P, 2 * BLK, B], F32).ap()
    land = nc.alloc_sbuf_tensor("landing", [P, BLK, B], F32).ap()
    wraw = nc.alloc_sbuf_tensor("w_raw", [P, 4, HALF], F32).ap()
    whi = nc.alloc_sbuf_tensor("w_hi", [P, 4, HALF], F32R).ap()
    wlo = nc.alloc_sbuf_tensor("w_lo", [P, 4, HALF], F32R).ap()
    xhi = nc.alloc_sbuf_tensor("x_hi", [P, 4, B], F32R).ap()
    xlo = nc.alloc_sbuf_tensor("x_lo", [P, 4, B], F32R).ap()
    bias = nc.alloc_sbuf_tensor("bias", [P, 6, BLK], F32).ap()
    idx_i = nc.alloc_sbuf_tensor("idx_i", [P, 6], I32).ap()
    idx_m = nc.alloc_sbuf_tensor("idx_m", [P, 6], I32).ap()
    idx_f = nc.alloc_sbuf_tensor("idx_f", [P, 6], F32).ap()
    hit = nc.alloc_sbuf_tensor("hit", [P, FIELDS, 6], F32).ap()
    rem = nc.alloc_sbuf_tensor("rem", [P, FIELDS], F32).ap()
    coef = nc.alloc_sbuf_tensor("coef", [P, FIELDS], F32).ap()
    count = nc.alloc_sbuf_tensor("count", [P, 1], F32).ap()
    inv = nc.alloc_sbuf_tensor("inv", [P, 1], F32).ap()
    btot = nc.alloc_sbuf_tensor("b_total", [P, BLK], F32).ap()
    psum = [nc.alloc_psum_tensor(f"acc{b}", [P, B], F32).ap() for b in range(BANKS)]

    rest = land
    res_t = xt[:, BLK:2 * BLK, :]
    res = xt[:, 0:BLK, :].rearrange("p a b -> p (a b)").rearrange("p (j h) -> p j h", h=SPAN)

    sem = nc.alloc_semaphore
    not_landed = [sem(f"not_half_landed{n}") for n in range(4)]
    half_landed = [sem(f"field_half_landed{n}") for n in range(2)]
    transposed = sem("blocks_transposed")
    w_landed = [sem(f"weight_pair_landed{n}") for n in range(2)]
    small_landed = sem("biases_landed")
    idx_landed = sem("indices_landed")
    w_hi_ready, w_lo_ready = sem("w_hi_ready"), sem("w_lo_ready")
    x_hi_ready, x_lo_ready = sem("x_hi_ready"), sem("x_lo_ready")
    units_done = sem("units_done")
    banks_done = sem("banks_done")
    banks_free = sem("banks_free")
    and_added = sem("and_hidden_added")
    step = sem("vector_steps")
    rest_step = sem("rest_steps")
    res_t_ready = sem("res_t_ready")
    res_ready = sem("res_ready")
    stored = sem("out_stored")

    block = nc.Block()
    block.__enter__()

    @block.sync
    def _(sp):
        slots = Slots(sp, not_idx)

        def load_half(field, half, to, landed):
            for i in range(NQ):
                src = x[:, bass.ds(field, 1), i * SPAN + half * LAND:i * SPAN + (half + 1) * LAND]
                sp.dma_start(to[i * Q:(i + 1) * Q],
                             src.rearrange("(j c) one h -> c (j one) h", c=Q)).then_inc(landed, DMA)

        def not_half(n):
            to = hid[:, n * HB:(n + 1) * HB, :].rearrange("p a b -> p (a b)")
            field = slots.n0 if n % 2 == 0 else second_field
            load_half(field, n // 2, to.rearrange("p (j h) -> p j h", h=LAND), not_landed[n])

        def field_half(c, wait):
            to = land[:, (c % 2) * HB:(c % 2 + 1) * HB, :].rearrange("p a b -> p (a b)")
            if wait:
                sp.wait_ge(transposed, 4 * BLK // 2 + HB * (c - 1))
            load_half(slots.field(2 + c // 2), c % 2, to.rearrange("p (j h) -> p j h", h=LAND),
                      half_landed[c % 2])

        def spread_rows(w, row, cols, slot):
            for i in range(NQ):
                sp.dma_start(wraw[i * Q:(i + 1) * Q, 2 * slot:2 * slot + 2, :],
                             w[bass.ds(row + i * SPAN, 2 * Q), cols].rearrange("(u r) n -> r u n", r=Q)
                             ).then_inc(w_landed[slot], DMA)

        def both_halves(w, row, slot):
            for i in range(NQ):
                sp.dma_start(wraw[i * Q:(i + 1) * Q, 2 * slot:2 * slot + 2, :],
                             w[bass.ds(row + i * SPAN, Q), :].rearrange("r (u n) -> r u n", u=2)
                             ).then_inc(w_landed[slot], DMA)

        def plain_rows(w, row, half, slot):
            for u in range(2):
                for p in range(0, P, P // 2):
                    src = w[bass.ds(row + u * P + p, P // 2), :].rearrange("k (i n) -> k i n", i=NQ)
                    sp.dma_start(wraw[p:p + P // 2, 2 * slot + u, :].rearrange("k (i n) -> k i n", i=NQ),
                                 src[:, :, half * LAND:(half + 1) * LAND]).then_inc(w_landed[slot], DMA)

        def raw_free(pair):
            sp.wait_ge(w_hi_ready, 2 * pair - 2)
            sp.wait_ge(w_lo_ready, 2 * pair - 2)

        second_field = slots.field(1)
        not_half(0)
        not_half(1)
        spread_rows(wn1, 0, slice(0, HALF), 0)
        spread_rows(wn1, 2 * Q, slice(0, HALF), 1)
        not_half(2)
        not_half(3)
        for pair in (2, 3):
            raw_free(pair)
            spread_rows(wn1, 2 * Q * pair, slice(0, HALF), pair % 2)
        for quad in range(6):
            for n in range(2):
                pair = 4 + 2 * quad + n
                raw_free(pair)
                if pair < 8:
                    spread_rows(wn1, 2 * Q * (pair - 4), slice(HALF, H), n)
                else:
                    plain_rows(wn2, 2 * P * (pair % 4), pair // 4 - 2, n)
                field_half(2 * quad + n, quad > 0)
        for half in range(2):
            with sp.Fori(0, BLK // 2) as quad:
                for member in range(2):
                    raw_free(AND0 // 2 + half * BLK + 2 * quad + member)
                    spread_rows(wa1, member * H + 2 * Q * quad, slice(half * HALF, (half + 1) * HALF),
                                member)
        with sp.Fori(0, BLK) as blk:
            for member in range(2):
                raw_free(OR0 // 2 + 2 * blk + member)
                both_halves(wo1, member * H + Q * blk, member)
        for half in range(2):
            for n, w in enumerate((wa2, wo2)):
                with sp.Fori(0, BLK // 4) as quad:
                    for u in range(2):
                        raw_free(OUT0 // 2 + half * BLK + n * (BLK // 2) + 2 * quad + u)
                        plain_rows(w, 4 * P * quad + 2 * P * u, half, u)
        for half in range(2):
            sp.wait_ge(res_ready, HB * (half + 1))
            for i in range(NQ):
                h = half * LAND
                sp.dma_start(
                    out[:, i * SPAN + h:i * SPAN + h + LAND].rearrange("(j c) h -> c j h", c=Q),
                    res[i * Q:(i + 1) * Q, :, h:h + LAND]).then_inc(stored, DMA)
        sp.wait_ge(stored, 2 * NQ * DMA)

    def wait_bank(eng, before, bank, size, last_unit):
        if bank < size - 1:
            eng.wait_ge(banks_done, before + bank + 1)
        else:
            eng.wait_ge(units_done, last_unit + 1)

    def w_tiles(spread_cols, j):
        tiles = [t[:, j, :] for t in (wraw, whi, wlo)]
        if spread_cols:
            tiles[0] = tiles[0].rearrange("p (i b r) -> p i b r", i=NQ, b=HB)
            tiles[1:] = [t.rearrange("p (b i r) -> p i b r", i=NQ, b=HB) for t in tiles[1:]]
        return tiles

    def as_f32(ap):
        return ap.bitcast(F32)

    @block.scalar
    def _(act):
        for n, (b, spread) in enumerate(((bn1, False), (bn2, True), (ba1, False), (ba2, True),
                                         (bo1, False), (bo2, True))):
            if spread:
                for i in range(NQ):
                    act.dma_start(bias[i * Q:(i + 1) * Q, n, :],
                                  b[i * SPAN:(i + 1) * SPAN].rearrange("(b r) -> r b", r=Q)
                                  ).then_inc(small_landed, DMA)
            else:
                act.dma_start(bias[:, n, :], b.rearrange("(b p) -> p b", p=P)
                              ).then_inc(small_landed, DMA)
        act.dma_start(idx_i[:, 0:4], and_pairs.rearrange("(o a) b -> o (a b)", o=1)
                      .to_broadcast([P, 4])).then_inc(idx_landed, DMA)
        act.dma_start(idx_i[:, 4:6], or_pairs.to_broadcast([P, 2])).then_inc(idx_landed, DMA)
        slots = Slots(act, not_idx)
        member = [[slots.slot(slots.index(and_pairs[s:s + 1, m:m + 1])) for m in range(2)] for s in range(2)]
        or_member = [slots.slot(slots.index(or_pairs[0:1, m:m + 1])) for m in range(2)]
        act.wait_ge(small_landed, (3 + 3 * NQ) * DMA)
        nc.scalar.activation(count[:, :], bias[:, 0, 0:1], ACT.Tanh).then_inc(banks_free, FREE0)

        def w_hi(unit, j, spread, wait, landed):
            act.wait_ge(w_landed[j // 2], landed)
            if wait:
                act.wait_ge(units_done, unit - 3)
            raw, hi, _ = w_tiles(spread, j)
            nc.scalar.copy(hi, raw).then_inc(w_hi_ready, 1)

        def x_hi(src, slot):
            nc.scalar.copy(xhi[:, slot, :], src).then_inc(x_hi_ready, 1)

        def landed(unit):
            return PAIR * (unit >> 2) + PAIR

        def two_set_unit(unit, j, spread, tiles, wait, w_wait):
            w_hi(unit, j, spread, w_wait, landed(unit))
            if wait:
                act.wait_ge(units_done, unit - 1)
            for s in range(2):
                x_hi(tiles[s], 2 * (j % 2) + s)

        def drain(group, unit):
            layer, half = divmod(group, 2)
            for b in range(HB):
                for s in range(2):
                    bank = 2 * b + s
                    blk = half * HB + b
                    wait_bank(act, (BANKS - 1) * group, bank, BANKS, unit - 1)
                    if layer == 1:
                        to = xt[:, bass.ds(slots.second * BLK + blk, 1), :][:, 0, :] if s else xt[:, blk, :]
                    else:
                        to = hid[:, s * BLK + blk, :]
                    nc.scalar.activation(to, psum[bank], ACT.Tanh if layer == 1 else ACT.Relu,
                                         bias=bias[:, layer, blk:blk + 1]).then_inc(banks_free, 1)

        def drain_or():
            for half in range(2):
                for b in range(HB):
                    blk = half * HB + b
                    wait_bank(act, (BANKS - 1) * GROUPS_2 + (HB - 1) * half, b, HB, OUT0 - 2 + half)
                    if blk == 0:
                        act.wait_ge(and_added, BLK)
                    nc.scalar.activation(hid[:, BLK + blk, :], psum[blk], ACT.Relu,
                                         bias=bias[:, 4, blk:blk + 1]).then_inc(banks_free, 1)

        def field_tile(slot, blk):
            return xt[:, bass.ds(slot * BLK + blk, 1), :][:, 0, :]

        for group in range(4):
            for k in range(BLK):
                unit = group * BLK + k
                if group < 2:
                    tiles = [xt[:, k, :], field_tile(slots.second, k)]
                    if group == 0:
                        act.wait_ge(transposed, 2 * k + 2)
                else:
                    tiles = [hid[:, k, :], hid[:, BLK + k, :]]
                    act.wait_ge(banks_free, FREE0 + (BANKS if k < HB else 2 * BANKS))
                two_set_unit(unit, k % 4, group >= 2, tiles, unit >= 2, unit >= 4)
                if k == 0 and group > 0:
                    drain(group - 1, unit)

        for half in range(2):
            group = 4 + half
            act.wait_ge(banks_free, FREE0 + 3 * BANKS)
            act.wait_ge(transposed, BLK * FIELDS)

            def and_quad(quad, first):
                for j in range(4):
                    m, k = divmod(j, 2)
                    unit = AND0 + half * 2 * BLK + 4 * quad + j
                    two_set_unit(unit, j, False,
                                 [field_tile(member[s][m], 2 * quad + k) for s in range(2)], True, True)
                    if first and j == 0:
                        drain(group - 1, unit)

            and_quad(0, True)
            act.wait_ge(banks_free, FREE0 + 4 * BANKS)
            with act.Fori(1, BLK // 2) as quad:
                and_quad(quad, False)

        def or_steps(oct, first):
            for n in range(4):
                unit = OR0 + 8 * oct + 2 * n
                for u in range(2):
                    w_hi(unit + u, 2 * (n % 2) + u, False, True, landed(unit))
                    if u == 0:
                        act.wait_ge(units_done, OR0 - 1 + n // 2 if first else OR0 - 6 + 8 * oct + 2 * n)
                        x_hi(field_tile(or_member[n % 2], 2 * oct + n // 2), n)
                if first and n == 0:
                    drain(5, unit)

        or_steps(0, True)
        with act.Fori(1, 4) as oct:
            or_steps(oct, False)

        def out_quad(half, quad, blk0, first):
            for j in range(4):
                unit = OUT0 + half * 2 * BLK + 4 * quad + j
                w_hi(unit, j, True, True, landed(unit))
                if first and half == 0:
                    act.wait_ge(units_done, OUT0 - 6 + 2 * j)
                else:
                    act.wait_ge(units_done, unit - 3)
                src = hid[:, bass.ds(4 * quad + j, 1), :][:, 0, :] if not first else hid[:, j, :]
                x_hi(src, j)
                if first and half == 0 and j == 0:
                    drain_or()

        act.wait_ge(and_added, BLK)
        for half in range(2):
            out_quad(half, 0, 0, True)
            if half == 0:
                act.wait_ge(banks_free, FREE0 + 7 * BANKS)
            with act.Fori(1, 4) as quad:
                out_quad(half, quad, 0, False)

    @block.vector
    def _(dve):
        slots = Slots(dve, not_idx)
        member = [[slots.slot(slots.index(and_pairs[s:s + 1, m:m + 1])) for m in range(2)] for s in range(2)]
        or_member = [slots.slot(slots.index(or_pairs[0:1, m:m + 1])) for m in range(2)]

        def field_tile(slot, blk):
            return xt[:, bass.ds(slot * BLK + blk, 1), :][:, 0, :]

        def transpose_block(src, half, b, to):
            nc.vector.transpose(to.rearrange("p (j c) -> p j c", c=Q),
                                src[:, :, b * Q:(b + 1) * Q]).then_inc(transposed, 1)

        def w_lo(unit, j, spread):
            dve.wait_ge(w_hi_ready, unit + 1)
            raw, hi, lo = w_tiles(spread, j)
            nc.vector.tensor_tensor(lo, raw, as_f32(hi), ALU.subtract).then_inc(w_lo_ready, 1)

        def x_lo(tile, src, slot):
            dve.wait_ge(x_hi_ready, tile + 1)
            nc.vector.tensor_tensor(xlo[:, slot, :], src, as_f32(xhi[:, slot, :]), ALU.subtract
                                    ).then_inc(x_lo_ready, 1)

        def two_set_unit(unit, j, spread, tiles):
            w_lo(unit, j, spread)
            for s in range(2):
                x_lo(2 * unit + s, tiles[s], 2 * (j % 2) + s)

        def landing(place, half):
            return place[:, half * HB:(half + 1) * HB, :].rearrange("p a b -> p (a b)").rearrange(
                "p (j h) -> p j h", h=LAND)

        def weights_of_rest():
            steps = [0]

            def then(ins):
                steps[0] += 1
                ins.then_inc(step, 1)
                dve.wait_ge(step, steps[0])

            dve.wait_ge(idx_landed, 2 * DMA)
            then(nc.vector.tensor_scalar(idx_m[:, :], idx_i[:, :], FIELDS - 1, None, ALU.bitwise_and))
            then(nc.vector.tensor_copy(idx_f[:, :], idx_m[:, :]))
            for f in range(FIELDS):
                ins = nc.vector.tensor_scalar(hit[:, f, :], idx_f[:, :], float(f), None, ALU.is_equal)
            then(ins)
            then(nc.vector.tensor_reduce(rem[:, :], hit[:, :, :], axis=AX.X, op=ALU.max))
            then(nc.vector.tensor_scalar(rem[:, :], rem[:, :], -1.0, 1.0, ALU.mult, ALU.add))
            then(nc.vector.tensor_reduce(inv[:, :], rem[:, :], axis=AX.X, op=ALU.add))
            then(nc.vector.tensor_scalar(inv[:, :], inv[:, :], 3.0, None, ALU.add))
            then(nc.vector.reciprocal(inv[:, :], inv[:, :]))
            then(nc.vector.tensor_scalar(rem[:, :], rem[:, :], inv[:, 0:1], None, ALU.mult))
            for s in range(FIELDS):
                ins = nc.vector.tensor_copy(coef[:, s:s + 1], rem[:, bass.ds(slots.field(s), 1)])
            dve.wait_ge(small_landed, (3 + 3 * NQ) * DMA)
            then(nc.vector.scalar_tensor_tensor(btot[:, :], bias[:, 3, :], 2.0, bias[:, 5, :],
                                                ALU.mult, ALU.add))
            then(nc.vector.tensor_scalar(btot[:, :], btot[:, :], inv[:, 0:1], None, ALU.mult))

        def rest_ops(blk, first, last, done):
            to = rest[:, bass.ds(blk, 1), :][:, 0, :]
            for s in range(first, last):
                src = xt[:, bass.ds(s * BLK + blk, 1), :][:, 0, :]
                if s == 0:
                    ins = nc.vector.tensor_scalar(to, src, coef[:, 0:1], btot[:, bass.ds(blk, 1)],
                                                  ALU.mult, ALU.add)
                else:
                    dve.wait_ge(rest_step, done + s)
                    ins = nc.vector.scalar_tensor_tensor(to, src, coef[:, s:s + 1], to,
                                                         ALU.mult, ALU.add)
                ins.then_inc(rest_step, 1)

        def add_and(half):
            for b in range(HB):
                blk = half * HB + b
                dve.wait_ge(banks_free, FREE0 + (4 + half) * BANKS + 2 * b + 2)
                nc.vector.tensor_tensor(hid[:, blk, :], hid[:, blk, :], hid[:, BLK + blk, :], ALU.add
                                        ).then_inc(and_added, 1)

        for group in range(4):
            for k in range(BLK):
                unit = group * BLK + k
                if group == 0:
                    for s in range(2):
                        n = 2 * (k // HB) + s
                        if k % HB == 0:
                            dve.wait_ge(not_landed[n], PAIR)
                        transpose_block(landing(hid, n), k // HB, k % HB, xt[:, s * BLK + k, :])
                if group < 2:
                    tiles = [xt[:, k, :], field_tile(slots.second, k)]
                else:
                    tiles = [hid[:, k, :], hid[:, BLK + k, :]]
                two_set_unit(unit, k % 4, group >= 2, tiles)
                if group == 0 and k == BLK - 1:
                    weights_of_rest()
                if group > 0:
                    c = 2 * ((unit - BLK) // 4) + k % 4 // 2
                    if k % 2 == 0:
                        dve.wait_ge(half_landed[c % 2], PAIR * (c // 2 + 1))
                    for b in range(2 * (k % 2), 2 * (k % 2) + 2):
                        transpose_block(landing(land, c % 2), c % 2, b,
                                        xt[:, (2 + c // 2) * BLK + (c % 2) * HB + b, :])

        for half in range(2):
            def and_quad(quad, first):
                blk = half * HB + quad
                for j in range(4):
                    m, k = divmod(j, 2)
                    unit = AND0 + half * 2 * BLK + 4 * quad + j
                    two_set_unit(unit, j, False,
                                 [field_tile(member[s][m], 2 * quad + k) for s in range(2)])
                    if j > 0:
                        if first and half == 0 and j == 1:
                            dve.wait_ge(banks_free, FREE0 + 4 * BANKS)
                        rest_ops(blk, 3 * j - 3, min(3 * j, FIELDS), FIELDS * blk)
                    if first and half == 1 and j == 2:
                        add_and(0)

            and_quad(0, True)
            with dve.Fori(1, BLK // 2) as quad:
                and_quad(quad, False)

        def or_steps(oct, first):
            for n in range(4):
                unit = OR0 + 8 * oct + 2 * n
                w_lo(unit, 2 * (n % 2), False)
                x_lo(X_OR0 + 4 * oct + n, field_tile(or_member[n % 2], 2 * oct + n // 2), n)
                w_lo(unit + 1, 2 * (n % 2) + 1, False)
                if first and n == 1:
                    add_and(1)

        or_steps(0, True)
        with dve.Fori(1, 4) as oct:
            or_steps(oct, False)

        def finish(half):
            for b in range(HB):
                blk = half * HB + b
                wait_bank(dve, (BANKS - 1) * GROUPS_2 + (HB - 1) * (2 + half), b, HB,
                          OUT0 + 2 * BLK * (half + 1) - 1)
                nc.vector.scalar_tensor_tensor(res_t[:, blk, :], psum[blk], inv[:, 0:1], rest[:, blk, :],
                                               ALU.mult, ALU.add).then_inc(res_t_ready, 1)
                dve.wait_ge(res_t_ready, blk + 1)
                nc.vector.transpose(res[:, :, blk * Q:(blk + 1) * Q],
                                    res_t[:, blk, :].rearrange("p (j c) -> p j c", c=Q)
                                    ).then_inc(res_ready, 1)

        def out_quad(half, quad, first):
            for j in range(4):
                unit = OUT0 + half * 2 * BLK + 4 * quad + j
                w_lo(unit, j, True)
                src = hid[:, bass.ds(4 * quad + j, 1), :][:, 0, :] if not first else hid[:, j, :]
                x_lo(X_OUT0 + half * 2 * BLK + 4 * quad + j, src, j)
                if first and half == 1 and j == 1:
                    finish(0)

        for half in range(2):
            out_quad(half, 0, True)
            with dve.Fori(1, 4) as quad:
                out_quad(half, quad, False)
        finish(1)

    @block.tensor
    def _(pe):
        def products(bank, w, b, xs, start, stop):
            cols = slice(b * P, (b + 1) * P)
            nc.tensor.matmul(psum[bank], whi[:, w, cols], xhi[:, xs, :], start=start, stop=False)
            nc.tensor.matmul(psum[bank], whi[:, w, cols], xlo[:, xs, :], start=False, stop=False)
            return nc.tensor.matmul(psum[bank], wlo[:, w, cols], xhi[:, xs, :], start=False, stop=stop)

        def unit_waits(unit, tiles):
            pe.wait_ge(w_hi_ready, unit + 1)
            pe.wait_ge(x_hi_ready, tiles)
            pe.wait_ge(w_lo_ready, unit + 1)
            pe.wait_ge(x_lo_ready, tiles)

        def two_set_unit(unit, j, free, stop):
            unit_waits(unit, 2 * unit + 2)
            for b in range(HB):
                for s in range(2):
                    bank = 2 * b + s
                    if free is not None:
                        pe.wait_ge(banks_free, free + bank)
                    last = products(bank, j, b, 2 * (j % 2) + s, free is not None, stop)
                    if stop and bank < BANKS - 1:
                        last.then_inc(banks_done, 1)
            return last

        def quad_2(unit0, free, stop):
            for j in range(4):
                last = two_set_unit(unit0 + j, j, free if j == 0 else None, stop and j == 3)
                last.then_inc(units_done, 1)

        with pe.Fori(0, 4) as group:
            quad_2(BLK * group, BANKS * group + 1, False)
            quad_2(BLK * group + 4, None, True)
        with pe.Fori(0, 2) as half:
            quad_2(AND0 + 2 * BLK * half, 4 * BANKS + BANKS * half + 1, False)
            with pe.Fori(1, BLK // 2 - 1) as quad:
                quad_2(AND0 + 2 * BLK * half + 4 * quad, None, False)
            quad_2(AND0 + 2 * BLK * half + 12, None, True)

        def or_oct(oct, first, stop):
            for n in range(4):
                for u in range(2):
                    unit = OR0 + 8 * oct + 2 * n + u
                    unit_waits(unit, X_OR0 + 4 * oct + n + 1)
                    for b in range(HB):
                        bank = u * HB + b
                        if first and n == 0:
                            pe.wait_ge(banks_free, 6 * BANKS + bank + 1)
                        last = products(bank, 2 * (n % 2) + u, b, n, first and n == 0, stop and n == 3)
                        if stop and n == 3 and b < HB - 1:
                            last.then_inc(banks_done, 1)
                    last.then_inc(units_done, 1)

        or_oct(0, True, False)
        with pe.Fori(1, 3) as oct:
            or_oct(oct, False, False)
        or_oct(3, False, True)

        def out_quad(half, quad, first):
            for j in range(4):
                unit = OUT0 + 2 * BLK * half + 4 * quad + j
                unit_waits(unit, X_OUT0 + 2 * BLK * half + 4 * quad + j + 1)
                for b in range(HB):
                    bank = half * HB + b
                    if first and j == 0:
                        pe.wait_ge(banks_free, 7 * BANKS + bank + 1)
                    last = products(bank, j, b, j, first and j == 0, False)
                last.then_inc(units_done, 1)

        def out_last_quad(half):
            unit = OUT0 + 2 * BLK * half + 12
            for b in range(HB):
                for j in range(4):
                    if b == 0:
                        unit_waits(unit + j, X_OUT0 + 2 * BLK * half + 12 + j + 1)
                    last = products(half * HB + b, j, b, j, False, j == 3)
                    if b == HB - 1:
                        last.then_inc(units_done, 1)
                if b < HB - 1:
                    last.then_inc(banks_done, 1)

        for half in range(2):
            out_quad(half, 0, True)
            with pe.Fori(1, 3) as quad:
                out_quad(half, quad, False)
            out_last_quad(half)

    block.__exit__(None, None, None)


INPUTS = ["r_field_vectors", "L0_rec_Wn1", "L0_rec_bn1", "L0_rec_Wn2", "L0_rec_bn2", "L0_rec_Wa1",
          "L0_rec_ba1", "L0_rec_Wa2", "L0_rec_ba2", "L0_rec_Wo1", "L0_rec_bo1", "L0_rec_Wo2",
          "L0_rec_bo2", "L0_rec_not_idx", "L0_rec_and_pairs", "L0_rec_or_pairs"]


def kernel(**inputs):
    import concourse.bacc as bacc
    from concourse.bass_utils import run_bass_kernel_spmd

    nc = bacc.Bacc("TRN2", target_bir_lowering=False, num_devices=1, dynamic_dma_scratch_size=1024)
    arrays, args = {}, []
    for name in INPUTS:
        a = np.ascontiguousarray(inputs[name])
        arrays[f"in_{name}"] = a
        args.append(nc.dram_tensor(f"in_{name}", a.shape, mybir.dt.from_np(a.dtype),
                                   kind="ExternalInput").ap())
    args.append(nc.dram_tensor("out_0", (B, H), F32, kind="ExternalOutput").ap())
    with nc.allow_non_contiguous_dma(reason="six bias vectors of 4 KiB, one element per partition"):
        build(nc, *args)
    r = run_bass_kernel_spmd(nc, [arrays], core_ids=[0])
    return r.results[0]["out_0"]
```

```python
import numpy as np
import concourse.bass as bass
import concourse.mybir as mybir

F32 = mybir.dt.float32
F32R = mybir.dt.float32r
I32 = mybir.dt.int32
ALU = mybir.AluOpType
ACT = mybir.ActivationFunctionType
AX = mybir.AxisListType

P = 128
Q = 32
NQ = P // Q
FIELDS = 8
H = 1024
B = 512
BLK = H // P
SPAN = H // NQ
HALF = H // 2
HB = BLK // 2
LAND = SPAN // 2
DMA = 16
PAIR = 4 * DMA

NOT_UNITS = 2 * BLK
AND0 = 2 * NOT_UNITS
OR0 = AND0 + 4 * BLK
OUT0 = OR0 + 4 * BLK
UNITS = OUT0 + 4 * BLK
WARM_UP = 6
PARTS = (0, BLK // 2, BLK)
X_OR0 = 2 * OR0
X_OUT0 = X_OR0 + 2 * BLK
BANKS = 8
GROUPS_2 = 6
FREE0 = BANKS


def ne(a, b):
    return (((a - b) & (FIELDS - 1)) + FIELDS - 1) >> 3


class Slots:

    made = 0

    def __init__(self, eng, not_idx):
        self.eng = eng
        raw = [self.register() for _ in range(2)]
        eng.load(raw, not_idx)
        self.raw = [eng.snap(r) for r in raw]
        self.n0 = self.small(self.raw[0] & (FIELDS - 1))

    def second_index(self):
        self.n1 = self.small(self.raw[1] & (FIELDS - 1))
        self.second = self.small(ne(self.n0, self.n1))

    def field1(self):
        return self.small(self.n1 * self.second + ne(self.n0, 1) * (1 - self.second))

    def prepare(self):
        self.p1 = self.small(self.swap0(self.n1) + 1 - self.second)

    def register(self):
        Slots.made += 1
        return self.eng.alloc_register(f"slots_{Slots.made}")

    def small(self, v):
        reg = self.register()
        self.eng.reg_mov(reg, v)
        return self.eng.snap(reg, min_val=0, max_val=FIELDS - 1)

    def index(self, ap):
        return self.small(self.eng.value_load(ap) & (FIELDS - 1))

    def swap0(self, f):
        return self.small(f * ne(f, self.n0) + self.n0 * (1 - ne(f, 0)))

    def swap1(self, x):
        return self.small(x + (self.p1 - 1) * (ne(x, self.p1) - ne(x, 1)))

    def slot(self, field):
        return self.swap1(self.swap0(field))

    def field(self, slot):
        return self.swap0(self.swap1(slot))


def build(nc, x, wn1, bn1, wn2, bn2, wa1, ba1, wa2, ba2, wo1, bo1, wo2, bo2,
          not_idx, and_pairs, or_pairs, out):
    not_idx = not_idx.rearrange("(o n) -> o n", o=1)
    xt = nc.alloc_sbuf_tensor("fields_t", [P, FIELDS * BLK, B], F32).ap()
    hid = nc.alloc_sbuf_tensor("hidden_t", [P, 2 * BLK, B], F32).ap()
    land = nc.alloc_sbuf_tensor("landing", [P, BLK, B], F32).ap()
    wraw = nc.alloc_sbuf_tensor("w_raw", [P, 4, HALF], F32).ap()
    whi = nc.alloc_sbuf_tensor("w_hi", [P, 4, HALF], F32R).ap()
    wlo = nc.alloc_sbuf_tensor("w_lo", [P, 4, HALF], F32R).ap()
    xhi = nc.alloc_sbuf_tensor("x_hi", [P, 4, B], F32R).ap()
    xlo = nc.alloc_sbuf_tensor("x_lo", [P, 4, B], F32R).ap()
    bias = nc.alloc_sbuf_tensor("bias", [P, BLK, BLK], F32).ap()
    bias_rows = nc.alloc_sbuf_tensor("bias_rows", [Q, 2, P], F32).ap()
    idx_i = nc.alloc_sbuf_tensor("idx_i", [P, 6], I32).ap()
    idx_m = nc.alloc_sbuf_tensor("idx_m", [P, 6], I32).ap()
    idx_f = nc.alloc_sbuf_tensor("idx_f", [P, 6], F32).ap()
    hit = nc.alloc_sbuf_tensor("hit", [P, FIELDS, 6], F32).ap()
    rem = nc.alloc_sbuf_tensor("rem", [P, FIELDS], F32).ap()
    coef = nc.alloc_sbuf_tensor("coef", [P, FIELDS], F32).ap()
    first_tanh = nc.alloc_sbuf_tensor("first_tanh", [P, 1], F32).ap()
    inv = nc.alloc_sbuf_tensor("inv", [P, 1], F32).ap()
    btot = nc.alloc_sbuf_tensor("b_total", [P, BLK], F32).ap()
    psum = [nc.alloc_psum_tensor(f"acc{b}", [P, B], F32).ap() for b in range(BANKS)]

    rest = land
    res_t = xt[:, BLK:2 * BLK, :]
    res = xt[:, 0:BLK, :].rearrange("p a b -> p (a b)").rearrange("p (j h) -> p j h", h=SPAN)

    not_land = [hid[:, s * BLK:(s + 1) * BLK, :].rearrange("p a b -> p (a b)")
                .rearrange("p (j h) -> p j h", h=SPAN) for s in range(2)]
    half_land = [land[:, n * HB:(n + 1) * HB, :].rearrange("p a b -> p (a b)")
                 .rearrange("p (j h) -> p j h", h=LAND) for n in range(2)]

    sem = nc.alloc_semaphore
    not_landed = [sem(f"not_part_landed{n}") for n in range(2 * (len(PARTS) - 1))]
    half_landed = [sem(f"field_half_landed{n}") for n in range(2)]
    transposed = sem("blocks_transposed")
    w_landed = [sem(f"weight_pair_landed{n}") for n in range(2)]
    small_landed = sem("biases_landed")
    idx_landed = sem("indices_landed")
    zeros_ready = sem("zeros_ready")
    bias_cleared = sem("bias_rows_cleared")
    bias_ready = sem("biases_ready")
    rem_ready = sem("rem_ready")
    coef_ready = sem("coef_ready")
    w_hi_ready, w_lo_ready = sem("w_hi_ready"), sem("w_lo_ready")
    x_hi_ready, x_lo_ready = sem("x_hi_ready"), sem("x_lo_ready")
    units_done = sem("units_done")
    banks_done = sem("banks_done")
    banks_free = sem("banks_free")
    and_added = sem("and_hidden_added")
    step = sem("vector_steps")
    rest_step = sem("rest_steps")
    res_t_ready = sem("res_t_ready")
    res_ready = sem("res_ready")
    stored = sem("out_stored")

    block = nc.Block()
    block.__enter__()

    def load_part(eng, field, first, last, to, landed):
        for i in range(NQ):
            src = x[:, bass.ds(field, 1), i * SPAN + first * Q:i * SPAN + last * Q]
            eng.dma_start(to[i * Q:(i + 1) * Q],
                          src.rearrange("(j c) one h -> c (j one) h", c=Q)).then_inc(landed, DMA)

    def load_not_part(eng, part, s, field):
        first, last = PARTS[part:part + 2]
        load_part(eng, field, first, last, not_land[s][:, :, first * Q:last * Q],
                  not_landed[2 * part + s])

    def spread_rows(eng, w, row, cols, slot):
        for i in range(NQ):
            eng.dma_start(wraw[i * Q:(i + 1) * Q, 2 * slot:2 * slot + 2, :],
                         w[bass.ds(row + i * SPAN, 2 * Q), cols].rearrange("(u r) n -> r u n", r=Q)
                         ).then_inc(w_landed[slot], DMA)

    @block.sync
    def _(sp):
        def field_half(slots, c, wait):
            if wait:
                sp.wait_ge(transposed, 2 * BLK + HB * (c - 1))
            load_part(sp, slots.field(2 + c // 2), HB * (c % 2), HB * (c % 2 + 1), half_land[c % 2],
                      half_landed[c % 2])

        def both_halves(w, row, slot):
            for i in range(NQ):
                sp.dma_start(wraw[i * Q:(i + 1) * Q, 2 * slot:2 * slot + 2, :],
                             w[bass.ds(row + i * SPAN, Q), :].rearrange("r (u n) -> r u n", u=2)
                             ).then_inc(w_landed[slot], DMA)

        def plain_rows(w, row, half, slot):
            for u in range(2):
                for p in range(0, P, P // 2):
                    src = w[bass.ds(row + u * P + p, P // 2), :].rearrange("k (i n) -> k i n", i=NQ)
                    sp.dma_start(wraw[p:p + P // 2, 2 * slot + u, :].rearrange("k (i n) -> k i n", i=NQ),
                                 src[:, :, half * LAND:(half + 1) * LAND]).then_inc(w_landed[slot], DMA)

        def raw_free(pair):
            sp.wait_ge(w_hi_ready, 2 * pair - 2)
            sp.wait_ge(w_lo_ready, 2 * pair - 2)

        slots = Slots(sp, not_idx)
        load_not_part(sp, 0, 0, slots.n0)
        slots.second_index()
        field1 = slots.field1()
        load_not_part(sp, 0, 1, field1)
        spread_rows(sp, wn1, 2 * Q, slice(0, HALF), 1)
        for part in range(1, len(PARTS) - 1):
            load_not_part(sp, part, 0, slots.n0)
            load_not_part(sp, part, 1, field1)
        for pair in (2, 3):
            raw_free(pair)
            spread_rows(sp, wn1, 2 * Q * pair, slice(0, HALF), pair % 2)
        slots.prepare()
        for quad in range(6):
            for n in range(2):
                pair = 4 + 2 * quad + n
                raw_free(pair)
                if pair < 8:
                    spread_rows(sp, wn1, 2 * Q * (pair - 4), slice(HALF, H), n)
                else:
                    plain_rows(wn2, 2 * P * (pair % 4), pair // 4 - 2, n)
                field_half(slots, 2 * quad + n, quad > 0)
        for half in range(2):
            with sp.Fori(0, BLK // 2) as quad:
                for member in range(2):
                    raw_free(AND0 // 2 + half * BLK + 2 * quad + member)
                    spread_rows(sp, wa1, member * H + 2 * Q * quad, slice(half * HALF, (half + 1) * HALF),
                                member)
        with sp.Fori(0, BLK) as blk:
            for member in range(2):
                raw_free(OR0 // 2 + 2 * blk + member)
                both_halves(wo1, member * H + Q * blk, member)
        for half in range(2):
            for n, w in enumerate((wa2, wo2)):
                with sp.Fori(0, BLK // 4) as quad:
                    for u in range(2):
                        raw_free(OUT0 // 2 + half * BLK + n * (BLK // 2) + 2 * quad + u)
                        plain_rows(w, 4 * P * quad + 2 * P * u, half, u)
        for first, last in ((0, HB), (HB, HB + 2), (HB + 2, BLK)):
            sp.wait_ge(res_ready, last)
            for i in range(NQ):
                sp.dma_start(
                    out[:, i * SPAN + first * Q:i * SPAN + last * Q].rearrange("(j c) h -> c j h", c=Q),
                    res[i * Q:(i + 1) * Q, :, first * Q:last * Q]).then_inc(stored, DMA)
        sp.wait_ge(stored, 3 * NQ * DMA)

    @block.gpsimd
    def _(pool):
        nc.gpsimd.memset(land[:, 0, :], 0.0).then_inc(zeros_ready, 1)
        nc.gpsimd.memset(bias_rows[:, :, :], 0.0).then_inc(bias_cleared, 1)
        pool.wait_ge(bias_cleared, 1)
        for n, (b, spread) in enumerate(((bn1, False), (bn2, True), (ba1, False), (ba2, True),
                                         (bo1, False), (bo2, True))):
            rows = bias_rows[n % NQ * BLK:(n % NQ + 1) * BLK, n // NQ, :].rearrange("b (i r) -> b i r", r=Q)
            order = "(i b r) -> b i r" if spread else "(b i r) -> b i r"
            pool.dma_start(rows, b.rearrange(order, i=NQ, r=Q)).then_inc(small_landed, DMA)
        pool.dma_start(idx_i[:, 0:4], and_pairs.rearrange("(o a) b -> o (a b)", o=1)
                       .to_broadcast([P, 4])).then_inc(idx_landed, DMA)
        pool.dma_start(idx_i[:, 4:6], or_pairs.to_broadcast([P, 2])).then_inc(idx_landed, DMA)
        slots = Slots(pool, not_idx)
        slots.second_index()
        slots.prepare()
        pool.wait_ge(rem_ready, 1)
        for s in range(FIELDS):
            nc.gpsimd.tensor_copy(coef[:, s:s + 1], rem[:, bass.ds(slots.field(s), 1)]
                                  ).then_inc(coef_ready, 1)

    def wait_bank(eng, before, bank, size, last_unit):
        if bank < size - 1:
            eng.wait_ge(banks_done, before + bank + 1)
        else:
            eng.wait_ge(units_done, last_unit + 1)

    def w_tiles(spread_cols, j):
        tiles = [t[:, j, :] for t in (wraw, whi, wlo)]
        if spread_cols:
            tiles[0] = tiles[0].rearrange("p (i b r) -> p i b r", i=NQ, b=HB)
            tiles[1:] = [t.rearrange("p (b i r) -> p i b r", i=NQ, b=HB) for t in tiles[1:]]
        return tiles

    def find_member(slots, member, n):
        if n == 0:
            slots.prepare()
        if n < 4:
            member[n] = slots.slot(slots.index(and_pairs[n // 2:n // 2 + 1, n % 2:n % 2 + 1]))
        elif n < 6:
            member[n] = slots.slot(slots.index(or_pairs[0:1, n - 4:n - 3]))

    def field_tile(slot, blk):
        return xt[:, bass.ds(slot * BLK + blk, 1), :][:, 0, :]

    def as_f32(ap):
        return ap.bitcast(F32)

    @block.scalar
    def _(act):
        spread_rows(act, wn1, 0, slice(0, HALF), 0)
        slots = Slots(act, not_idx)
        slots.second_index()
        member = {}
        act.wait_ge(zeros_ready, 1)
        nc.scalar.activation(first_tanh[:, :], land[:, 0, 0:1], ACT.Tanh).then_inc(banks_free, FREE0)

        def w_hi(unit, j, spread, wait, landed):
            act.wait_ge(w_landed[j // 2], landed)
            if wait:
                act.wait_ge(units_done, unit - 3)
            raw, hi, _ = w_tiles(spread, j)
            nc.scalar.copy(hi, raw).then_inc(w_hi_ready, 1)

        def x_hi(src, slot):
            nc.scalar.copy(xhi[:, slot, :], src).then_inc(x_hi_ready, 1)

        def landed(unit):
            return PAIR * (unit >> 2) + PAIR

        def two_set_unit(unit, j, spread, tiles, wait, w_wait, turned=0):
            w_hi(unit, j, spread, w_wait, landed(unit))
            if wait:
                act.wait_ge(units_done, unit - 1)
            for s in range(2):
                if turned:
                    act.wait_ge(transposed, turned + s)
                x_hi(tiles[s], 2 * (j % 2) + s)

        def drain(group, unit):
            layer, half = divmod(group, 2)
            for b in range(HB):
                for s in range(2):
                    bank = 2 * b + s
                    blk = half * HB + b
                    wait_bank(act, (BANKS - 1) * group, bank, BANKS, unit - 1)
                    if layer == 1:
                        if s:
                            act.wait_ge(banks_free, FREE0 + BANKS * group + bank)
                        to = field_tile(slots.second, blk) if s else xt[:, blk, :]
                    else:
                        to = hid[:, s * BLK + blk, :]
                    nc.scalar.activation(to, psum[bank], ACT.Tanh if layer == 1 else ACT.Relu,
                                         bias=bias[:, layer, blk:blk + 1]).then_inc(banks_free, 1)

        def drain_or():
            for half in range(2):
                for b in range(HB):
                    blk = half * HB + b
                    wait_bank(act, (BANKS - 1) * GROUPS_2 + (HB - 1) * half, b, HB, OUT0 - 2 + half)
                    if blk == 0:
                        act.wait_ge(and_added, BLK)
                    nc.scalar.activation(hid[:, BLK + blk, :], psum[blk], ACT.Relu,
                                         bias=bias[:, 4, blk:blk + 1]).then_inc(banks_free, 1)

        for group in range(4):
            for k in range(BLK):
                unit = group * BLK + k
                if group < 2:
                    tiles = [xt[:, k, :], field_tile(slots.second, k)]
                else:
                    tiles = [hid[:, k, :], hid[:, BLK + k, :]]
                    act.wait_ge(banks_free, FREE0 + (BANKS if k < HB else 2 * BANKS))
                two_set_unit(unit, k % 4, group >= 2, tiles, unit >= 2, unit >= 4,
                             2 * k + 1 if group == 0 else 0)
                if k == 0 and group > 0:
                    if group == 1:
                        act.wait_ge(bias_ready, 2 * NQ)
                    drain(group - 1, unit)
                if group == 1 and k >= 2:
                    find_member(slots, member, k - 2)

        for half in range(2):
            group = 4 + half
            act.wait_ge(banks_free, FREE0 + 3 * BANKS)
            act.wait_ge(transposed, BLK * FIELDS)

            def and_quad(quad, first):
                for j in range(4):
                    m, k = divmod(j, 2)
                    unit = AND0 + half * 2 * BLK + 4 * quad + j
                    two_set_unit(unit, j, False,
                                 [field_tile(member[2 * s + m], 2 * quad + k) for s in range(2)], True, True)
                    if first and j == 0:
                        drain(group - 1, unit)

            and_quad(0, True)
            act.wait_ge(banks_free, FREE0 + 4 * BANKS)
            with act.Fori(1, BLK // 2) as quad:
                and_quad(quad, False)

        def or_steps(oct, first):
            for n in range(4):
                unit = OR0 + 8 * oct + 2 * n
                for u in range(2):
                    w_hi(unit + u, 2 * (n % 2) + u, False, True, landed(unit))
                    if u == 0:
                        act.wait_ge(units_done, OR0 - 1 + n // 2 if first else OR0 - 6 + 8 * oct + 2 * n)
                        x_hi(field_tile(member[4 + n % 2], 2 * oct + n // 2), n)
                if first and n == 0:
                    drain(GROUPS_2 - 1, unit)

        or_steps(0, True)
        with act.Fori(1, 4) as oct:
            or_steps(oct, False)

        def out_quad(half, quad, first):
            for j in range(4):
                unit = OUT0 + half * 2 * BLK + 4 * quad + j
                w_hi(unit, j, True, True, landed(unit))
                if first and half == 0:
                    act.wait_ge(units_done, OUT0 - 6 + 2 * j)
                else:
                    act.wait_ge(units_done, unit - 3)
                src = hid[:, bass.ds(4 * quad + j, 1), :][:, 0, :] if not first else hid[:, j, :]
                x_hi(src, j)
                if first and half == 0 and j == 0:
                    drain_or()

        act.wait_ge(and_added, BLK)
        for half in range(2):
            out_quad(half, 0, True)
            if half == 0:
                act.wait_ge(banks_free, FREE0 + 7 * BANKS)
            with act.Fori(1, 4) as quad:
                out_quad(half, quad, False)

    @block.vector
    def _(dve):
        slots = Slots(dve, not_idx)
        slots.second_index()
        member = {}

        def transpose_block(src, b, to):
            nc.vector.transpose(to.rearrange("p (j c) -> p j c", c=Q),
                                src[:, :, b * Q:(b + 1) * Q]).then_inc(transposed, 1)

        def w_lo(unit, j, spread):
            dve.wait_ge(w_hi_ready, unit + 1)
            raw, hi, lo = w_tiles(spread, j)
            nc.vector.tensor_tensor(lo, raw, as_f32(hi), ALU.subtract).then_inc(w_lo_ready, 1)

        def x_lo(tile, src, slot):
            dve.wait_ge(x_hi_ready, tile + 1)
            nc.vector.tensor_tensor(xlo[:, slot, :], src, as_f32(xhi[:, slot, :]), ALU.subtract
                                    ).then_inc(x_lo_ready, 1)

        def two_set_unit(unit, j, spread, tiles):
            w_lo(unit, j, spread)
            for s in range(2):
                x_lo(2 * unit + s, tiles[s], 2 * (j % 2) + s)

        def weights_of_rest():
            steps = [0]

            def then(ins):
                steps[0] += 1
                ins.then_inc(step, 1)
                dve.wait_ge(step, steps[0])

            dve.wait_ge(idx_landed, 2 * DMA)
            then(nc.vector.tensor_scalar(idx_m[:, :], idx_i[:, :], FIELDS - 1, None, ALU.bitwise_and))
            then(nc.vector.tensor_copy(idx_f[:, :], idx_m[:, :]))
            for f in range(FIELDS):
                ins = nc.vector.tensor_scalar(hit[:, f, :], idx_f[:, :], float(f), None, ALU.is_equal)
            then(ins)
            then(nc.vector.tensor_reduce(rem[:, :], hit[:, :, :], axis=AX.X, op=ALU.max))
            then(nc.vector.tensor_scalar(rem[:, :], rem[:, :], -1.0, 1.0, ALU.mult, ALU.add))
            then(nc.vector.tensor_reduce(inv[:, :], rem[:, :], axis=AX.X, op=ALU.add))
            then(nc.vector.tensor_scalar(inv[:, :], inv[:, :], 3.0, None, ALU.add))
            then(nc.vector.reciprocal(inv[:, :], inv[:, :]))
            then(nc.vector.tensor_scalar(rem[:, :], rem[:, :], inv[:, 0:1], None, ALU.mult))
            dve.wait_ge(bias_ready, 2 * NQ)
            then(nc.vector.scalar_tensor_tensor(btot[:, :], bias[:, 3, :], 2.0, bias[:, 5, :],
                                                ALU.mult, ALU.add))
            nc.vector.tensor_scalar(btot[:, :], btot[:, :], inv[:, 0:1], None, ALU.mult
                                    ).then_inc(rem_ready, 1)

        def turn_negated(k, s):
            if k in PARTS:
                dve.wait_ge(not_landed[2 * PARTS.index(k) + s], PAIR)
            transpose_block(not_land[s], k, xt[:, s * BLK + k, :])

        def turn_biases():
            dve.wait_ge(small_landed, 6 * DMA)
            for i in range(NQ):
                for g in range(2):
                    nc.vector.transpose(
                        bias[i * Q:(i + 1) * Q, g * NQ:(g + 1) * NQ, :].rearrange("p n b -> p (n b)"),
                        bias_rows[:, g, i * Q:(i + 1) * Q]).then_inc(bias_ready, 1)

        def rest_ops(blk, first, last, done):
            to = rest[:, bass.ds(blk, 1), :][:, 0, :]
            for s in range(first, last):
                src = xt[:, bass.ds(s * BLK + blk, 1), :][:, 0, :]
                if s == 0:
                    ins = nc.vector.tensor_scalar(to, src, coef[:, 0:1], btot[:, bass.ds(blk, 1)],
                                                  ALU.mult, ALU.add)
                else:
                    dve.wait_ge(rest_step, done + s)
                    ins = nc.vector.scalar_tensor_tensor(to, src, coef[:, s:s + 1], to,
                                                         ALU.mult, ALU.add)
                ins.then_inc(rest_step, 1)

        def add_and(half):
            for b in range(HB):
                blk = half * HB + b
                dve.wait_ge(banks_free, FREE0 + (4 + half) * BANKS + 2 * b + 2)
                nc.vector.tensor_tensor(hid[:, blk, :], hid[:, blk, :], hid[:, BLK + blk, :], ALU.add
                                        ).then_inc(and_added, 1)

        for group in range(4):
            for k in range(BLK):
                unit = group * BLK + k
                if group < 2:
                    tiles = [xt[:, k, :], field_tile(slots.second, k)]
                else:
                    tiles = [hid[:, k, :], hid[:, BLK + k, :]]
                if unit > 0:
                    two_set_unit(unit, k % 4, group >= 2, tiles)
                else:
                    turn_negated(0, 0)
                    w_lo(0, 0, False)
                    x_lo(0, tiles[0], 0)
                    turn_negated(0, 1)
                    turn_negated(1, 0)
                    x_lo(1, tiles[1], 1)
                    turn_negated(1, 1)
                if group == 0 and 0 < k < BLK - 1:
                    for s in range(2):
                        turn_negated(k + 1, s)
                if unit == 2:
                    turn_biases()
                if group == 0 and k == BLK - 3:
                    weights_of_rest()
                if group == 1 and k >= 2:
                    find_member(slots, member, k - 2)
                if group > 0:
                    c = 2 * ((unit - BLK) // 4) + k % 4 // 2
                    if k % 2 == 0:
                        dve.wait_ge(half_landed[c % 2], PAIR * (c // 2 + 1))
                    for b in range(2 * (k % 2), 2 * (k % 2) + 2):
                        transpose_block(half_land[c % 2], b,
                                        xt[:, (2 + c // 2) * BLK + (c % 2) * HB + b, :])

        for half in range(2):
            def and_quad(quad, first):
                blk = half * HB + quad
                for j in range(4):
                    m, k = divmod(j, 2)
                    unit = AND0 + half * 2 * BLK + 4 * quad + j
                    two_set_unit(unit, j, False,
                                 [field_tile(member[2 * s + m], 2 * quad + k) for s in range(2)])
                    if j > 0:
                        if first and half == 0 and j == 1:
                            dve.wait_ge(banks_free, FREE0 + 4 * BANKS)
                            dve.wait_ge(coef_ready, FIELDS)
                        rest_ops(blk, 3 * j - 3, min(3 * j, FIELDS), FIELDS * blk)
                    if first and half == 1 and j == 2:
                        add_and(0)

            and_quad(0, True)
            with dve.Fori(1, BLK // 2) as quad:
                and_quad(quad, False)

        def or_steps(oct, first):
            for n in range(4):
                unit = OR0 + 8 * oct + 2 * n
                w_lo(unit, 2 * (n % 2), False)
                x_lo(X_OR0 + 4 * oct + n, field_tile(member[4 + n % 2], 2 * oct + n // 2), n)
                w_lo(unit + 1, 2 * (n % 2) + 1, False)
                if first and n == 1:
                    add_and(1)

        or_steps(0, True)
        with dve.Fori(1, 4) as oct:
            or_steps(oct, False)

        def finish(half):
            for b in range(HB):
                blk = half * HB + b
                wait_bank(dve, (BANKS - 1) * GROUPS_2 + (HB - 1) * (2 + half), b, HB,
                          OUT0 + 2 * BLK * (half + 1) - 1)
                nc.vector.scalar_tensor_tensor(res_t[:, blk, :], psum[blk], inv[:, 0:1], rest[:, blk, :],
                                               ALU.mult, ALU.add).then_inc(res_t_ready, 1)
                dve.wait_ge(res_t_ready, blk + 1)
                nc.vector.transpose(res[:, :, blk * Q:(blk + 1) * Q],
                                    res_t[:, blk, :].rearrange("p (j c) -> p j c", c=Q)
                                    ).then_inc(res_ready, 1)

        def out_quad(half, quad, first):
            for j in range(4):
                unit = OUT0 + half * 2 * BLK + 4 * quad + j
                w_lo(unit, j, True)
                src = hid[:, bass.ds(4 * quad + j, 1), :][:, 0, :] if not first else hid[:, j, :]
                x_lo(X_OUT0 + half * 2 * BLK + 4 * quad + j, src, j)
                if first and half == 1 and j == 1:
                    finish(0)

        for half in range(2):
            out_quad(half, 0, True)
            with dve.Fori(1, 4) as quad:
                out_quad(half, quad, False)
        finish(1)

    @block.tensor
    def _(pe):
        def product(bank, w, b, x_tile, start, stop):
            return nc.tensor.matmul(psum[bank], w[:, b * P:(b + 1) * P], x_tile, start=start, stop=stop)

        def products(bank, w, b, xs, start, stop):
            product(bank, whi[:, w], b, xhi[:, xs, :], start, False)
            product(bank, whi[:, w], b, xlo[:, xs, :], False, False)
            return product(bank, wlo[:, w], b, xhi[:, xs, :], False, stop)

        def hi_waits(unit, tiles):
            pe.wait_ge(w_hi_ready, unit + 1)
            pe.wait_ge(x_hi_ready, tiles)

        def lo_waits(unit, tiles):
            pe.wait_ge(w_lo_ready, unit + 1)
            pe.wait_ge(x_lo_ready, tiles)

        def unit_waits(unit, tiles):
            hi_waits(unit, tiles)
            lo_waits(unit, tiles)

        def first_unit():
            for s in range(2):
                hi_waits(0, s + 1)
                for b in range(HB):
                    product(2 * b + s, whi[:, 0], b, xhi[:, s, :], True, False)
                lo_waits(0, s + 1)
                for b in range(HB):
                    product(2 * b + s, whi[:, 0], b, xlo[:, s, :], False, False)
                    last = product(2 * b + s, wlo[:, 0], b, xhi[:, s, :], False, False)
            last.then_inc(units_done, 1)

        def two_set_unit(unit, j, free, stop):
            unit_waits(unit, 2 * unit + 2)
            tiles = [2 * (j % 2) + s for s in range(2)]
            for b in range(HB):
                for s in range(2):
                    if free is not None:
                        pe.wait_ge(banks_free, free + 2 * b + s)
                    product(2 * b + s, whi[:, j], b, xhi[:, tiles[s], :], free is not None, False)
                    product(2 * b + s, whi[:, j], b, xlo[:, tiles[s], :], False, False)
                for s in range(2):
                    bank = 2 * b + s
                    last = product(bank, wlo[:, j], b, xhi[:, tiles[s], :], False, stop)
                    if stop and bank < BANKS - 1:
                        last.then_inc(banks_done, 1)
            last.then_inc(units_done, 1)

        def quad_2(unit0, free, stop):
            for j in range(4):
                two_set_unit(unit0 + j, j, free if j == 0 else None, stop and j == 3)

        pe.wait_ge(zeros_ready, 1)
        for _ in range(WARM_UP):
            nc.tensor.matmul(psum[0], land[:, 0, 0:P], land[:, 0, :], start=True, stop=True)
        pe.wait_ge(banks_free, FREE0)
        first_unit()
        for j in range(1, 4):
            two_set_unit(j, j, None, False)
        quad_2(4, None, True)
        with pe.Fori(1, 4) as group:
            quad_2(BLK * group, BANKS * group + 1, False)
            quad_2(BLK * group + 4, None, True)
        with pe.Fori(0, 2) as half:
            quad_2(AND0 + 2 * BLK * half, 4 * BANKS + BANKS * half + 1, False)
            with pe.Fori(1, BLK // 2 - 1) as quad:
                quad_2(AND0 + 2 * BLK * half + 4 * quad, None, False)
            quad_2(AND0 + 2 * BLK * half + 12, None, True)

        def or_oct(oct, first, stop):
            for n in range(4):
                for u in range(2):
                    unit = OR0 + 8 * oct + 2 * n + u
                    unit_waits(unit, X_OR0 + 4 * oct + n + 1)
                    for b in range(HB):
                        bank = u * HB + b
                        if first and n == 0:
                            pe.wait_ge(banks_free, 6 * BANKS + bank + 1)
                        last = products(bank, 2 * (n % 2) + u, b, n, first and n == 0, stop and n == 3)
                        if stop and n == 3 and b < HB - 1:
                            last.then_inc(banks_done, 1)
                    last.then_inc(units_done, 1)

        or_oct(0, True, False)
        with pe.Fori(1, 3) as oct:
            or_oct(oct, False, False)
        or_oct(3, False, True)

        def out_quad(half, quad, first, stop):
            for j in range(4):
                unit = OUT0 + 2 * BLK * half + 4 * quad + j
                unit_waits(unit, X_OUT0 + 2 * BLK * half + 4 * quad + j + 1)
                for b in range(HB):
                    bank = half * HB + b
                    if first and j == 0:
                        pe.wait_ge(banks_free, 7 * BANKS + bank + 1)
                    last = products(bank, j, b, j, first and j == 0, stop and j == 3)
                    if stop and j == 3 and b < HB - 1:
                        last.then_inc(banks_done, 1)
                last.then_inc(units_done, 1)

        out_quad(0, 0, True, False)
        with pe.Fori(1, 3) as quad:
            out_quad(0, quad, False, False)
        out_quad(0, 3, False, True)
        out_quad(1, 0, True, False)
        with pe.Fori(1, 3) as quad:
            out_quad(1, quad, False, False)
        unit = UNITS - 4
        for b in range(HB):
            for j in range(4):
                if b == 0:
                    unit_waits(unit + j, X_OUT0 + 4 * BLK - 4 + j + 1)
                last = products(HB + b, j, b, j, False, j == 3)
                if b == HB - 1:
                    last.then_inc(units_done, 1)
            if b < HB - 1:
                last.then_inc(banks_done, 1)

    block.__exit__(None, None, None)


INPUTS = ["r_field_vectors", "L0_rec_Wn1", "L0_rec_bn1", "L0_rec_Wn2", "L0_rec_bn2", "L0_rec_Wa1",
          "L0_rec_ba1", "L0_rec_Wa2", "L0_rec_ba2", "L0_rec_Wo1", "L0_rec_bo1", "L0_rec_Wo2",
          "L0_rec_bo2", "L0_rec_not_idx", "L0_rec_and_pairs", "L0_rec_or_pairs"]


def kernel(**inputs):
    import concourse.bacc as bacc
    from concourse.bass_utils import run_bass_kernel_spmd

    nc = bacc.Bacc("TRN2", target_bir_lowering=False, num_devices=1, dynamic_dma_scratch_size=2048)
    arrays, args = {}, []
    for name in INPUTS:
        a = np.ascontiguousarray(inputs[name])
        arrays[f"in_{name}"] = a
        args.append(nc.dram_tensor(f"in_{name}", a.shape, mybir.dt.from_np(a.dtype),
                                   kind="ExternalInput").ap())
    args.append(nc.dram_tensor("out_0", (B, H), F32, kind="ExternalOutput").ap())
    build(nc, *args)
    r = run_bass_kernel_spmd(nc, [arrays], core_ids=[0])
    return r.results[0]["out_0"]
```
